# Optimizing a Trainium2 kernel written in Bass

```python
import numpy as np
import jax
import jax.numpy as jnp

def _softmax(x, axis=-1):
    return jax.nn.softmax(x, axis=axis)

def _gelu(x):
    return jax.nn.gelu(x, approximate=True)

def _silu(x):
    return jax.nn.silu(x)

def _sigmoid(x):
    return jax.nn.sigmoid(x)

def _layernorm(x, axis=-1, eps=1e-05):
    m = jnp.mean(x, axis=axis, keepdims=True)
    v = jnp.var(x, axis=axis, keepdims=True)
    return (x - m) / jnp.sqrt(v + eps)

def _scatter_add(tgt, idx, src, axis=0):
    return tgt.at[idx].add(src)

def _segment_sum(src, seg, n):
    return jax.ops.segment_sum(src, seg, n)
kernel_name = 'mk_adj_preln_d1_adj_r2_568cc6'

def setup_inputs(seed: int=0):
    np.random.seed(seed)
    _w = jnp.asarray

    def _rec_inputs():
        import jax
        import jax.numpy as jnp
        _gk = jax.random.key(seed)
        x = 7.22e-05 + 1 * jax.random.normal(jax.random.fold_in(_gk, 1), (4096, 256), jnp.float32)
        _a = jax.random.bernoulli(jax.random.fold_in(_gk, 2), 0.000488281, (4096, 4096))
        _a = jnp.logical_or(_a, jnp.eye(4096, dtype=bool))
        _af = _a.astype(jnp.float32)
        _af = _af * jax.random.uniform(jax.random.fold_in(_gk, 3), (4096, 4096), jnp.float32, 0.05, 1)
        adj = _af
        return (x, adj)
    x, adj = _rec_inputs()

    def _L0_gnn_setup():
        import jax, jax.numpy as jnp
        import numpy as np
        N = 8192
        F_IN = 256
        F_OUT = 256
        key = jax.random.key(seed)
        k = jax.random.split(key, 6)
        h = jax.random.normal(k[0], (N, F_IN), dtype=jnp.float32)
        adj = jax.random.uniform(k[1], (N, N), dtype=jnp.float32)
        W_neigh = jax.random.normal(k[2], (F_OUT, F_IN), dtype=jnp.float32) * (1.0 / np.sqrt(F_IN))
        b_neigh = jax.random.normal(k[3], (F_OUT,), dtype=jnp.float32) * 0.01
        W_self = jax.random.normal(k[4], (F_OUT, F_IN), dtype=jnp.float32) * (1.0 / np.sqrt(F_IN))
        b_self = jax.random.normal(k[5], (F_OUT,), dtype=jnp.float32) * 0.01
        return {'h': h, 'adj': adj, 'W_neigh': W_neigh, 'b_neigh': b_neigh, 'W_self': W_self, 'b_self': b_self}
    _L0_gnn_all = _L0_gnn_setup()
    _L0_gnn_in = {k: v for k, v in _L0_gnn_all.items() if k in ('W_neigh', 'b_neigh', 'W_self', 'b_self')}
    del _L0_gnn_all
    return {'x': x, 'adj': adj, 'L0_gnn_W_neigh': _L0_gnn_in['W_neigh'], 'L0_gnn_b_neigh': _L0_gnn_in['b_neigh'], 'L0_gnn_W_self': _L0_gnn_in['W_self'], 'L0_gnn_b_self': _L0_gnn_in['b_self']}

def reference(x, adj, L0_gnn_W_neigh, L0_gnn_b_neigh, L0_gnn_W_self, L0_gnn_b_self):
    import jax
    import jax.numpy as jnp

    def _L0_gnn_ref(h, adj, W_neigh, b_neigh, W_self, b_self):
        import jax, jax.numpy as jnp
        import numpy as np
        N = 8192
        F_IN = 256
        F_OUT = 256
        deg = jnp.sum(adj, axis=1, keepdims=True) + 1e-05
        adj_norm = adj / deg
        h_neigh = adj_norm @ h
        out = h_neigh @ W_neigh.T + b_neigh + h @ W_self.T + b_self
        return jax.nn.relu(out)
    h = jnp.maximum(_layernorm(x, axis=-1), 0.0)
    x = x + _L0_gnn_ref(h, adj, L0_gnn_W_neigh, L0_gnn_b_neigh, L0_gnn_W_self, L0_gnn_b_self)
    return x

_drawn_inputs = setup_inputs


def setup_inputs(seed=0):
    import zlib

    import numpy as np

    out = dict(_drawn_inputs(seed))
    spreads = {}
    factors = {'L0_gnn_b_neigh': 8.0, 'L0_gnn_b_self': 8.0}
    for name, (base, spread) in spreads.items():
        noise = np.random.default_rng([zlib.crc32(name.encode()), seed]).standard_normal(out[name].shape)
        drawn = base * np.exp(spread * noise) if base else spread * noise
        out[name] = jnp.asarray(drawn.astype(out[name].dtype))
    for name, factor in factors.items():
        out[name] = (out[name] * factor).astype(out[name].dtype)
    return out
```

```python
from contextlib import ExitStack

import concourse.bass as bass
from concourse import mybir


P = 128
ALU = mybir.AluOpType
ACT = mybir.ActivationFunctionType
F32 = mybir.dt.float32
F32R = mybir.dt.float32r

LN_EPS = 1e-5
DEG_EPS = 1e-5

RING = 4
UJ = 2
UI = 4
SETS = 2


def gnn_layer(nc, x, adj, wn, ws, bn, bs, out):
    _, T, F = x.shape
    Q, U, _, _, _ = adj.shape
    KC = F // P
    PAIRS = T // 2
    QUADS = T // 4
    GW = F + 2
    GC = GW + F
    CHUNKS = U // RING
    assert U * UJ == T and Q * UI == T and U % RING == 0 and F == 2 * P

    with ExitStack() as ctx:
        def sb(name, shape, dt=F32):
            return ctx.enter_context(nc.sbuf_tensor(name, shape, dt))

        def sem(name):
            return ctx.enter_context(nc.semaphore(name))

        x_sb = sb("x_sb", [P, T, F])
        self_sb = sb("self_sb", [P, T, F])
        g_sb = sb("g_sb", [P, T, GC], F32R)
        adj_raw = sb("adj_raw", [P, RING, UJ, UI * P])
        adj_hi = sb("adj_hi", [P, RING, UJ, UI * P], F32R)
        adj_lo = sb("adj_lo", [P, RING, UJ, UI * P], F32R)
        w_raw = sb("w_raw", [P, KC, 2, F])
        w_hi = sb("w_hi", [P, KC, 2, F], F32R)
        w_lo = sb("w_lo", [P, KC, 2, F], F32R)
        h_sb = sb("h_sb", [P, 2, 2, F])
        scaled = h_sb[:, :, :, :].rearrange("p a b f -> p (a b) f")
        ht_hi = sb("ht_hi", [P, 2, 2, KC, P], F32R)
        ht_lo = sb("ht_lo", [P, 2, 2, KC, P], F32R)
        ident = sb("ident", [P, P])
        b_raw = sb("b_raw", [P, 2, F])
        b_sum = sb("b_sum", [P, 1, F])
        stats = sb("stats", [P, 4, 6])
        mv = sb("mv", [P, 4, 2])
        rstd = sb("rstd", [P, T])
        shift = sb("shift", [P, T])
        consts = sb("consts", [P, 3, 4])
        deg = sb("deg", [P, 2, UI])

        banks = ctx.enter_context(nc.psum_tensor("banks", [P, SETS * UI, 512], F32))
        small = [banks[:, 2 * s:2 * s + 2, :] for s in range(2)]
        turned = [banks[:, 4 + s, :] for s in range(2)]

        x_parts = [(0, 1), (1, 2), (2, 4), (4, QUADS)]
        s_x = [sem(f"x_loaded{n}") for n in range(len(x_parts))]
        s_w = sem("w_loaded")
        s_b = sem("b_loaded")
        s_raw = [sem(f"adj_raw_loaded{r}") for r in range(RING)]
        s_zero = sem("ident_zeroed")
        s_ident = sem("ident_ready")
        s_ones = sem("ones_ready")
        s_whi = sem("w_hi_ready")
        s_wlo = sem("w_lo_ready")
        s_bsum = sem("b_sum_ready")
        s_stats = sem("stats_done")
        s_mv = sem("mv_done")
        s_consts = sem("consts_ready")
        s_rstd = sem("rstd_step_done")
        s_shift = sem("shift_step_done")
        s_norm = sem("norm_ready")
        s_h = sem("h_ready")
        s_turned = sem("h_turned")
        s_hthi = sem("ht_hi_ready")
        s_htlo = sem("ht_lo_ready")
        s_small = sem("small_product_done")
        s_ghi = sem("g_hi_ready")
        s_glo = sem("g_lo_ready")
        s_taken = sem("results_taken")
        s_hi = sem("adj_hi_ready")
        s_lo = sem("adj_lo_ready")
        s_used = sem("adj_unit_used")
        s_deg = sem("deg_ready")
        s_rdeg = sem("rdeg_ready")
        s_scaled = sem("scaled_ready")
        s_relu = sem("relu_ready")
        s_final = sem("rows_final")
        s_out = sem("out_stored")

        block = ctx.enter_context(nc.Block())

        @block.sync
        def _(sp):
            def load_x(n):
                a, b = x_parts[n]
                sp.dma_start(x_sb[:, 4 * a:4 * b, :], x[:, 4 * a:4 * b, :]).then_inc(s_x[n], 16)

            def load_units(c, ring_full):
                for r in range(RING):
                    if ring_full:
                        sp.wait_ge(s_hi, RING * c + r - RING + 1)
                        sp.wait_ge(s_lo, RING * c + r - RING + 1)
                    sp.dma_start(adj_raw[:, r, :, :],
                                 adj_units[bass.ds(RING * c + r, 1), :, :, :].rearrange("u p a i -> p (u a) i")) \
                      .then_inc(s_raw[r], 16)

            adj_units = adj.rearrange("q u p a i -> (q u) p a i")
            load_x(0)
            sp.dma_start(w_raw[:, :, 0, :], wn).then_inc(s_w, 16)
            sp.dma_start(w_raw[:, :, 1, :], ws).then_inc(s_w, 16)
            load_x(1)
            sp.dma_start(b_raw[:, 0, :], bn.broadcast_to([P, F])).then_inc(s_b, 16)
            sp.dma_start(b_raw[:, 1, :], bs.broadcast_to([P, F])).then_inc(s_b, 16)
            load_x(2)
            load_x(3)
            load_units(0, False)
            with sp.Fori(1, Q * U // RING) as c:
                load_units(c, True)

        @block.gpsimd
        def _(pool):
            nc.gpsimd.memset(ident[:, :], 0.0).then_inc(s_zero, 1)
            pool.wait_ge(s_zero, 1)
            nc.gpsimd.affine_select(out=ident[:, :], in_=ident[:, :], compare_op=ALU.not_equal, fill=1.0,
                                    base=0, pattern=[[-1, P]], channel_multiplier=1).then_inc(s_ident, 1)
            nc.gpsimd.memset(g_sb[:, :, F:GW].bitcast(F32), 1.0).then_inc(s_ones, 1)

            for n, value in enumerate((LN_EPS, -0.5, -1.0)):
                nc.gpsimd.memset(consts[:, n, :], value).then_inc(s_consts, 1)
            pool.wait_ge(s_consts, 3)
            for n in range(QUADS):
                cols = slice(4 * n, 4 * n + 4)
                pool.wait_ge(s_mv, n + 1)
                nc.gpsimd.tensor_tensor(rstd[:, cols], mv[:, :, 1], consts[:, 0, :], ALU.add).then_inc(s_rstd, 1)
                pool.wait_ge(s_rstd, 2 * n + 1)
                nc.gpsimd.tensor_tensor(rstd[:, cols], rstd[:, cols], consts[:, 1, :], ALU.pow).then_inc(s_rstd, 1)
                pool.wait_ge(s_rstd, 2 * n + 2)
                nc.gpsimd.tensor_tensor(shift[:, cols], mv[:, :, 0], rstd[:, cols], ALU.mult).then_inc(s_shift, 1)
                pool.wait_ge(s_shift, n + 1)
                nc.gpsimd.tensor_tensor(shift[:, cols], shift[:, cols], consts[:, 2, :], ALU.mult).then_inc(s_norm, 1)

            for q in range(Q):
                rows = slice(q * UI, (q + 1) * UI)
                pool.wait_ge(s_relu, q + 1)
                nc.gpsimd.tensor_tensor(x_sb[:, rows, :], x_sb[:, rows, :], self_sb[:, rows, :], ALU.add) \
                  .then_inc(s_final, 1)
                pool.wait_ge(s_final, q + 1)
                pool.dma_start(out[:, rows, :], x_sb[:, rows, :]).then_inc(s_out, 16)
            pool.wait_ge(s_out, 16 * Q)

        @block.scalar
        def _(act):
            def normalise(p, s, slot_used):
                if slot_used:
                    act.wait_ge(s_turned, p - 1)
                for t in range(2):
                    col = bass.ds(2 * p + t, 1)
                    last = nc.scalar.activation(h_sb[:, s, t, :], x_sb[:, col, :].rearrange("p a f -> p (a f)"),
                                                ACT.Relu, bias=shift[:, col], scale=rstd[:, col])
                last.then_inc(s_h, 1)

            def turned_high(p, s, slot_used):
                act.wait_ge(s_turned, p + 1)
                if slot_used:
                    act.wait_ge(s_small, p - 1)
                nc.scalar.activation(ht_hi[:, s, :, :, :].rearrange("p a k i -> p (a k i)"), turned[s], ACT.Copy) \
                  .then_inc(s_hthi, 1)

            def g_high(p, s):
                act.wait_ge(s_small, p + 1)
                nc.scalar.activation(g_sb[:, bass.ds(2 * p, 2), 0:F], small[s][:, :, 0:F], ACT.Copy) \
                  .then_inc(s_ghi, 1)

            act.wait_ge(s_w, 32)
            nc.scalar.activation(w_hi[:, :, :, :], w_raw[:, :, :, :], ACT.Copy).then_inc(s_whi, 1)
            act.wait_ge(s_norm, 1)
            normalise(0, 0, False)
            normalise(1, 1, False)
            turned_high(0, 0, False)

            act.wait_ge(s_norm, 2)
            normalise(2, 0, True)
            turned_high(1, 1, False)
            g_high(0, 0)
            normalise(3, 1, True)
            turned_high(2, 0, True)
            g_high(1, 1)
            with act.Fori(1, QUADS - 1) as n:
                act.wait_ge(s_norm, n + 2)
                for s in range(2):
                    normalise(2 * n + s + 2, s, True)
                    turned_high(2 * n + s + 1, 1 - s, True)
                    g_high(2 * n + s, s)
            turned_high(PAIRS - 1, 1, True)
            g_high(PAIRS - 2, 0)
            g_high(PAIRS - 1, 1)

            def split_high(c, slot_used):
                for r in range(RING):
                    act.wait_ge(s_raw[r], 16 * (c + 1))
                    if slot_used:
                        act.wait_ge(s_used, RING * (c - 1) + r + 1)
                    nc.scalar.activation(adj_hi[:, r, :, :], adj_raw[:, r, :, :], ACT.Copy).then_inc(s_hi, 1)

            def scale_group(q, bank_set):
                act.wait_ge(s_rdeg, q + 1)
                act.wait_ge(s_taken, PAIRS + q)
                for b in range(UI):
                    last = nc.scalar.activation(scaled[:, b, :], banks[:, bank_set * UI + b, 0:F], ACT.Copy,
                                                scale=deg[:, 1, b:b + 1])
                last.then_inc(s_scaled, 1)

            def relu_group(q):
                rows = bass.ds(q * UI, UI)
                act.wait_ge(s_taken, PAIRS + q + 1)
                nc.scalar.activation(self_sb[:, rows, :], self_sb[:, rows, :], ACT.Relu).then_inc(s_relu, 1)

            def group(q, bank_set, first=False):
                split_high(CHUNKS * q, not first)
                if not first:
                    scale_group(q - 1, 1 - bank_set)
                split_high(CHUNKS * q + 1, True)
                split_high(CHUNKS * q + 2, True)
                if not first:
                    relu_group(q - 1)
                for c in range(3, CHUNKS):
                    split_high(CHUNKS * q + c, True)

            group(0, 0, first=True)
            group(1, 1)
            with act.Fori(1, Q // SETS) as n:
                for s in range(SETS):
                    group(SETS * n + s, s)
            scale_group(Q - 1, SETS - 1)
            relu_group(Q - 1)

        @block.vector
        def _(dve):
            def statistics(quad, between, first=False):
                if not first:
                    dve.wait_ge(s_mv, quad)
                for t in range(4):
                    last = nc.vector.bn_stats(stats[:, t, :],
                                              x_sb[:, bass.ds(4 * quad + t, 1), :].rearrange("p a f -> p (a f)"))
                last.then_inc(s_stats, 1)
                dve.wait_ge(s_stats, quad + 1)
                if not first:
                    dve.wait_ge(s_norm, quad)
                between()
                for t in range(4):
                    last = nc.vector.bn_aggr(mv[:, t, :], stats[:, t, :])
                last.then_inc(s_mv, 1)

            def turned_low(p, s, slot_used):
                dve.wait_ge(s_hthi, p + 1)
                if slot_used:
                    dve.wait_ge(s_small, p - 1)
                nc.vector.tensor_tensor(ht_lo[:, s, :, :, :].rearrange("p a k i -> p (a k i)"), turned[s],
                                        ht_hi[:, s, :, :, :].rearrange("p a k i -> p (a k i)").bitcast(F32),
                                        ALU.subtract).then_inc(s_htlo, 1)

            def g_low_and_self(p, s):
                tiles = bass.ds(2 * p, 2)
                dve.wait_ge(s_ghi, p + 1)
                nc.vector.tensor_tensor(g_sb[:, tiles, GW:GC], small[s][:, :, 0:F],
                                        g_sb[:, tiles, 0:F].bitcast(F32), ALU.subtract).then_inc(s_glo, 1)
                nc.vector.tensor_tensor(self_sb[:, tiles, :], small[s][:, :, F:2 * F],
                                        b_sum[:, :, :].broadcast_to([P, 2, F]), ALU.add).then_inc(s_taken, 1)

            def weights_low():
                dve.wait_ge(s_whi, 1)
                nc.vector.tensor_tensor(w_lo[:, :, :, :], w_raw[:, :, :, :], w_hi[:, :, :, :].bitcast(F32),
                                        ALU.subtract).then_inc(s_wlo, 1)

            dve.wait_ge(s_x[0], 16)
            statistics(0, lambda: None, first=True)
            weights_low()
            dve.wait_ge(s_x[1], 16)
            statistics(1, lambda: None)
            turned_low(0, 0, False)
            dve.wait_ge(s_b, 32)
            nc.vector.tensor_tensor(b_sum[:, 0, :], b_raw[:, 0, :], b_raw[:, 1, :], ALU.add).then_inc(s_bsum, 1)
            dve.wait_ge(s_bsum, 1)

            turned_low(1, 1, False)
            g_low_and_self(0, 0)
            for a, b in x_parts[2:]:
                dve.wait_ge(s_x[x_parts.index((a, b))], 16)
                with dve.Fori(a, b) as n:
                    statistics(n, lambda: turned_low(2 * n - 2, 0, True))
                    g_low_and_self(2 * n - 3, 1)
                    turned_low(2 * n - 1, 1, True)
                    g_low_and_self(2 * n - 2, 0)
            turned_low(PAIRS - 2, 0, True)
            g_low_and_self(PAIRS - 3, 1)
            turned_low(PAIRS - 1, 1, True)
            g_low_and_self(PAIRS - 2, 0)
            g_low_and_self(PAIRS - 1, 1)

            def split_low(c, slot_used):
                for r in range(RING):
                    dve.wait_ge(s_hi, RING * c + r + 1)
                    if slot_used:
                        dve.wait_ge(s_used, RING * (c - 1) + r + 1)
                    nc.vector.tensor_tensor(adj_lo[:, r, :, :], adj_raw[:, r, :, :],
                                            adj_hi[:, r, :, :].bitcast(F32), ALU.subtract).then_inc(s_lo, 1)

            def degrees(q, bank_set, first=False):
                dve.wait_ge(s_used, U * (q + 1))
                nc.vector.tensor_scalar(deg[:, 0, :], banks[:, bank_set * UI:(bank_set + 1) * UI, F], DEG_EPS,
                                        None, ALU.add).then_inc(s_deg, 1)
                dve.wait_ge(s_deg, q + 1)
                if not first:
                    dve.wait_ge(s_scaled, q)
                nc.vector.reciprocal(deg[:, 1, :], deg[:, 0, :]).then_inc(s_rdeg, 1)

            def add_self(q):
                rows = bass.ds(q * UI, UI)
                dve.wait_ge(s_scaled, q + 1)
                nc.vector.tensor_tensor(self_sb[:, rows, :], self_sb[:, rows, :], scaled, ALU.add) \
                  .then_inc(s_taken, 1)

            def group(q, bank_set, first=False, second=False):
                split_low(CHUNKS * q, not first)
                if not first:
                    degrees(q - 1, 1 - bank_set, first=second)
                split_low(CHUNKS * q + 1, True)
                if not first:
                    add_self(q - 1)
                for c in range(2, CHUNKS):
                    split_low(CHUNKS * q + c, True)

            group(0, 0, first=True)
            group(1, 1, second=True)
            with dve.Fori(1, Q // SETS) as n:
                for s in range(SETS):
                    group(SETS * n + s, s)
            degrees(Q - 1, SETS - 1)
            add_self(Q - 1)

        @block.tensor
        def _(pe):
            def turn(p, s, slot_used):
                pe.wait_ge(s_h, p + 1)
                if slot_used:
                    pe.wait_ge(s_htlo, p - 1)
                for t in range(2):
                    for k in range(KC):
                        at = (t * KC + k) * P
                        last = nc.tensor.transpose(turned[s][:, at:at + P], h_sb[:, s, t, k * P:(k + 1) * P],
                                                   ident[:, :])
                last.then_inc(s_turned, 1)

            def small_product(p, s, slot_used):
                pe.wait_ge(s_htlo, p + 1)
                if slot_used:
                    pe.wait_ge(s_taken, p - 1)
                terms = [(h, w, k) for k in range(KC) for h, w in ((ht_hi, w_hi), (ht_hi, w_lo), (ht_lo, w_hi))]
                for t in range(2):
                    for n, (h, w, k) in enumerate(terms):
                        last = nc.tensor.matmul(small[s][:, t, :], h[:, s, t, k, :],
                                                w[:, k, :, :].rearrange("p a f -> p (a f)"),
                                                start=(n == 0), stop=(n == len(terms) - 1))
                last.then_inc(s_small, 1)

            pe.wait_ge(s_ident, 1)
            turn(0, 0, False)
            turn(1, 1, False)
            pe.wait_ge(s_wlo, 1)
            small_product(0, 0, False)
            turn(2, 0, True)
            small_product(1, 1, False)
            with pe.Fori(1, QUADS - 1) as n:
                for s in range(2):
                    turn(2 * n + s + 1, 1 - s, True)
                    small_product(2 * n + s, s, True)
            turn(PAIRS - 1, 1, True)
            small_product(PAIRS - 2, 0, True)
            small_product(PAIRS - 1, 1, True)

            def add_units(c, k, bank_set, first=False, last=False):
                for r in range(RING):
                    pe.wait_ge(s_lo, RING * c + r + 1)
                    for b in range(UI):
                        bank = banks[:, bank_set * UI + b, :]
                        for a in range(UJ):
                            j = bass.ds((RING * k + r) * UJ + a, 1)
                            g_hi = g_sb[:, j, 0:GW].rearrange("p a f -> p (a f)")
                            g_lo = g_sb[:, j, GW:GC].rearrange("p a f -> p (a f)")
                            hi = adj_hi[:, r, a, b * P:(b + 1) * P]
                            lo = adj_lo[:, r, a, b * P:(b + 1) * P]
                            start = first and r == 0 and a == 0
                            nc.tensor.matmul(bank[:, 0:GW], hi, g_hi, start=start, stop=False)
                            nc.tensor.matmul(bank[:, 0:F], hi, g_lo, start=False, stop=False)
                            stop = last and r == RING - 1 and a == UJ - 1
                            product = nc.tensor.matmul(bank[:, 0:GW], lo, g_hi, start=False, stop=stop)
                    product.then_inc(s_used, 1)

            pe.wait_ge(s_ones, 1)
            pe.wait_ge(s_taken, PAIRS)
            with pe.Fori(0, Q // SETS) as n:
                for s in range(SETS):
                    q = SETS * n + s
                    pe.wait_ge(s_taken, PAIRS + q - 1)
                    add_units(CHUNKS * q, 0, s, first=True)
                    with pe.Fori(1, CHUNKS - 1) as k:
                        add_units(CHUNKS * q + k, k, s)
                    add_units(CHUNKS * (q + 1) - 1, CHUNKS - 1, s, last=True)


def kernel(x, adj, L0_gnn_W_neigh, L0_gnn_b_neigh, L0_gnn_W_self, L0_gnn_b_self):
    import numpy as np
    import concourse.bacc as bacc
    from concourse.bass_utils import run_bass_kernel_spmd

    x, adj, wn, bn, ws, bs = (np.asarray(a) for a in (
        x, adj, L0_gnn_W_neigh, L0_gnn_b_neigh, L0_gnn_W_self, L0_gnn_b_self))
    N, F = x.shape
    T, Q, U = N // P, N // (UI * P), N // (UJ * P)

    def turned_weights(w):
        return w.T.reshape(F // P, P, F).transpose(1, 0, 2)

    arrays = {
        "x_in": x.reshape(T, P, F).transpose(1, 0, 2),
        "adj_in": adj.reshape(Q, UI * P, U, UJ, P).transpose(0, 2, 4, 3, 1),
        "w_neigh": turned_weights(wn),
        "w_self": turned_weights(ws),
        "b_neigh": bn.reshape(1, F),
        "b_self": bs.reshape(1, F),
    }
    arrays = {name: np.ascontiguousarray(a) for name, a in arrays.items()}
    nc = bacc.Bacc("TRN2", target_bir_lowering=False, num_devices=1)
    args = [nc.dram_tensor(name, a.shape, mybir.dt.from_np(a.dtype), kind="ExternalInput").ap()
            for name, a in arrays.items()]
    args.append(nc.dram_tensor("rows_out", (P, T, F), F32, kind="ExternalOutput").ap())
    gnn_layer(nc, *args)
    result = run_bass_kernel_spmd(nc, [arrays], core_ids=[0])
    rows = result.results[0]["rows_out"]
    return np.ascontiguousarray(rows.transpose(1, 0, 2)).reshape(N, F)
```

```python
from contextlib import ExitStack

import concourse.bass as bass
from concourse import mybir


P = 128
ALU = mybir.AluOpType
ACT = mybir.ActivationFunctionType
F32 = mybir.dt.float32
F32R = mybir.dt.float32r

LN_EPS = 1e-5
DEG_EPS = 1e-5

RING = 4
UJ = 2
UI = 4
SETS = 2


def gnn_layer(nc, x, adj, wn, ws, bn, bs, out):
    _, T, F = x.shape
    Q, U, _, _, _ = adj.shape
    KC = F // P
    PAIRS = T // 2
    QUADS = T // 4
    GW = F + 2
    GC = GW + F
    CHUNKS = U // RING
    assert U * UJ == T and Q * UI == T and U % RING == 0 and F == 2 * P

    with ExitStack() as ctx:
        def sb(name, shape, dt=F32):
            return ctx.enter_context(nc.sbuf_tensor(name, shape, dt))

        def sem(name):
            return ctx.enter_context(nc.semaphore(name))

        x_sb = sb("x_sb", [P, T, F])
        self_sb = sb("self_sb", [P, T, F])
        g_sb = sb("g_sb", [P, T, GC], F32R)
        adj_raw = sb("adj_raw", [P, RING, UJ, UI * P])
        adj_hi = sb("adj_hi", [P, RING, UJ, UI * P], F32R)
        adj_lo = sb("adj_lo", [P, RING, UJ, UI * P], F32R)
        w_raw = sb("w_raw", [P, KC, 2, F])
        w_hi = sb("w_hi", [P, KC, 2, F], F32R)
        w_lo = sb("w_lo", [P, KC, 2, F], F32R)
        h_sb = sb("h_sb", [P, 2, 2, F])
        scaled = h_sb[:, :, :, :].rearrange("p a b f -> p (a b) f")
        ht_hi, ht_lo = ([ring[:, RING // 2 + s // 2, s % 2, :].rearrange("p (a k i) -> p a k i", a=2, k=KC)
                         for s in range(4)] for ring in (adj_hi, adj_lo))
        ident = sb("ident", [P, P])
        b_raw = sb("b_raw", [P, 2, F])
        b_sum = sb("b_sum", [P, 1, F])
        stats = sb("stats", [P, 4, 6])
        mv = sb("mv", [P, 4, 2])
        rstd = sb("rstd", [P, T])
        shift = sb("shift", [P, T])
        consts = sb("consts", [P, 3, 4])
        deg = sb("deg", [P, 2, UI])

        banks = ctx.enter_context(nc.psum_tensor("banks", [P, SETS * UI, 512], F32))
        turned = [banks[:, s, :] for s in range(2)]
        small = [banks[:, UI + 2 * s:UI + 2 * s + 2, :] for s in range(2)]

        x_parts = [(0, 1), (1, 2), (2, 4), (4, QUADS)]
        s_x = [sem(f"x_loaded{n}") for n in range(len(x_parts))]
        s_w = sem("w_loaded")
        s_b = sem("b_loaded")
        s_raw = [sem(f"adj_raw_loaded{r}") for r in range(RING)]
        s_zero = sem("ident_zeroed")
        s_ident = sem("ident_ready")
        s_ones = sem("ones_ready")
        s_whi = sem("w_hi_ready")
        s_wlo = sem("w_lo_ready")
        s_bsum = sem("b_sum_ready")
        s_stats = sem("stats_done")
        s_mv = sem("mv_done")
        s_consts = sem("consts_ready")
        s_rstd = sem("rstd_step_done")
        s_shift = sem("shift_step_done")
        s_norm = sem("norm_ready")
        s_h = sem("h_ready")
        s_turned = sem("h_turned")
        s_hthi = sem("ht_hi_ready")
        s_htlo = sem("ht_lo_ready")
        s_small = sem("small_product_done")
        s_ghi = sem("g_hi_and_self_ready")
        s_self = sem("self_with_bias")
        s_taken = sem("results_taken")
        s_hi = sem("adj_hi_ready")
        s_lo = sem("adj_lo_ready")
        s_used = sem("adj_unit_used")
        s_bank = sem("bank_complete")
        s_deg = sem("deg_ready")
        s_rdeg = sem("rdeg_ready")
        s_scaled = sem("scaled_ready")
        s_relu = sem("relu_ready")
        s_final = sem("rows_final")
        s_last = sem("last_group_step")
        s_out = sem("out_stored")
        s_tail = sem("last_group_stored")

        block = ctx.enter_context(nc.Block())

        @block.sync
        def _(sp):
            def load_x(n):
                a, b = x_parts[n]
                sp.dma_start(x_sb[:, 4 * a:4 * b, :], x[:, 4 * a:4 * b, :]).then_inc(s_x[n], 16)

            def load_units(c, ring_full):
                for r in range(RING):
                    if ring_full:
                        sp.wait_ge(s_hi, RING * c + r - RING + 1)
                        sp.wait_ge(s_lo, RING * c + r - RING + 1)
                    sp.dma_start(adj_raw[:, r, :, :],
                                 adj_units[bass.ds(RING * c + r, 1), :, :, :].rearrange("u p a i -> p (u a) i")) \
                      .then_inc(s_raw[r], 16)

            adj_units = adj.rearrange("q u p a i -> (q u) p a i")
            load_x(0)
            load_x(1)
            sp.dma_start(w_raw[:, :, 0, :], wn).then_inc(s_w, 16)
            sp.dma_start(w_raw[:, :, 1, :], ws).then_inc(s_w, 16)
            sp.dma_start(b_raw[:, 0, :], bn.broadcast_to([P, F])).then_inc(s_b, 16)
            sp.dma_start(b_raw[:, 1, :], bs.broadcast_to([P, F])).then_inc(s_b, 16)
            load_x(2)
            load_x(3)
            load_units(0, False)
            with sp.Fori(1, Q * U // RING) as c:
                load_units(c, True)
            for half in range(2):
                rows = slice((Q - 1) * UI + 2 * half, (Q - 1) * UI + 2 * half + 2)
                sp.wait_ge(s_last, 8 * half + 8)
                sp.dma_start(out[:, rows, :], x_sb[:, rows, :]).then_inc(s_tail, 16)
            sp.wait_ge(s_tail, 32)

        @block.gpsimd
        def _(pool):
            nc.gpsimd.memset(ident[:, :], 0.0).then_inc(s_zero, 1)
            pool.wait_ge(s_zero, 1)
            nc.gpsimd.affine_select(out=ident[:, :], in_=ident[:, :], compare_op=ALU.not_equal, fill=1.0,
                                    base=0, pattern=[[-1, P]], channel_multiplier=1).then_inc(s_ident, 1)
            nc.gpsimd.memset(g_sb[:, :, F:GW].bitcast(F32), 1.0).then_inc(s_ones, 1)

            for n, value in enumerate((LN_EPS, -0.5, -1.0)):
                nc.gpsimd.memset(consts[:, n, :], value).then_inc(s_consts, 1)
            pool.wait_ge(s_consts, 3)

            def norm(quad):
                cols = slice(4 * quad, 4 * quad + 4)
                pool.wait_ge(s_mv, quad + 1)
                nc.gpsimd.tensor_tensor(rstd[:, cols], mv[:, :, 1], consts[:, 0, :], ALU.add).then_inc(s_rstd, 1)
                nc.gpsimd.tensor_tensor(shift[:, cols], mv[:, :, 0], consts[:, 2, :], ALU.mult).then_inc(s_shift, 1)
                pool.wait_ge(s_rstd, 2 * quad + 1)
                nc.gpsimd.tensor_tensor(rstd[:, cols], rstd[:, cols], consts[:, 1, :], ALU.pow).then_inc(s_rstd, 1)
                pool.wait_ge(s_rstd, 2 * quad + 2)
                pool.wait_ge(s_shift, quad + 1)
                nc.gpsimd.tensor_tensor(shift[:, cols], shift[:, cols], rstd[:, cols], ALU.mult).then_inc(s_norm, 1)

            for quad in range(3):
                norm(quad)
            for p in range(PAIRS):
                if p % 2 == 1 and (p + 5) // 2 < QUADS:
                    norm((p + 5) // 2)
                tiles = slice(2 * p, 2 * p + 2)
                if p == 0:
                    pool.wait_ge(s_bsum, 1)
                pool.wait_ge(s_ghi, p + 1)
                nc.gpsimd.tensor_tensor(self_sb[:, tiles, :], self_sb[:, tiles, :],
                                        b_sum[:, :, :].broadcast_to([P, 2, F]), ALU.add).then_inc(s_self, 1)

            for q in range(Q - 1):
                rows = slice(q * UI, (q + 1) * UI)
                pool.wait_ge(s_relu, q + 1)
                nc.gpsimd.tensor_tensor(x_sb[:, rows, :], x_sb[:, rows, :], self_sb[:, rows, :], ALU.add) \
                  .then_inc(s_final, 1)
                pool.wait_ge(s_final, q + 1)
                pool.dma_start(out[:, rows, :], x_sb[:, rows, :]).then_inc(s_out, 16)
            pool.wait_ge(s_out, 16 * (Q - 1))

        @block.scalar
        def _(act):
            def normalise(p, r, norms):
                act.wait_ge(s_norm, norms)
                if r is not None:
                    act.wait_ge(s_turned, p - 1)
                for t in range(2):
                    col = bass.ds(2 * p + t, 1)
                    last = nc.scalar.activation(h_sb[:, (r or 0) % 2 if r is not None else p % 2, t, :],
                                                x_sb[:, col, :].rearrange("p a f -> p (a f)"),
                                                ACT.Relu, bias=shift[:, col], scale=rstd[:, col])
                last.then_inc(s_h, 1)

            def turned_high(p, r, slot_used=True):
                act.wait_ge(s_turned, p + 1)
                if slot_used:
                    act.wait_ge(s_small, p - 3)
                nc.scalar.activation(ht_hi[r % 4], turned[r % 2].rearrange("p (a k i) -> p a k i", a=2, k=KC),
                                     ACT.Copy).then_inc(s_hthi, 1)

            def results(p, r):
                tiles = bass.ds(2 * p, 2)
                act.wait_ge(s_small, p + 1)
                nc.scalar.activation(g_sb[:, tiles, 0:F], small[r % 2][:, :, 0:F], ACT.Copy)
                nc.scalar.activation(self_sb[:, tiles, :], small[r % 2][:, :, F:2 * F], ACT.Copy).then_inc(s_ghi, 1)

            def split_unit(u, r, slot_used):
                if slot_used:
                    act.wait_ge(s_used, u - RING + 1)
                nc.scalar.activation(adj_hi[:, r, :, :], adj_raw[:, r, :, :], ACT.Copy).then_inc(s_hi, 1)

            act.wait_ge(s_w, 32)
            nc.scalar.activation(w_hi[:, :, :, :], w_raw[:, :, :, :], ACT.Copy).then_inc(s_whi, 1)
            normalise(0, None, 1)
            normalise(1, None, 1)
            turned_high(0, 0, slot_used=False)
            turned_high(1, 1, slot_used=False)
            normalise(2, 2, 2)

            def prepare(first_pair, position):
                for r in range(4):
                    p = first_pair + r
                    if position != "last" or r + 3 < 4:
                        normalise(p + 3, r + 3, first_pair // 2 + (r + 3) // 2 + 1)
                    if position != "last" or r + 2 < 4:
                        turned_high(p + 2, r + 2, slot_used=position != "first" or r + 2 >= 4)
                    else:
                        u = r - 2
                        act.wait_ge(s_raw[u], 16)
                        split_unit(u, u, False)
                    results(p, r)

            prepare(0, "first")
            with act.Fori(1, PAIRS // 4 - 1) as n:
                prepare(4 * n, "middle")
            prepare(PAIRS - 4, "last")

            def split_high(c, first=False):
                for r in range(2 if first else 0, RING):
                    act.wait_ge(s_raw[r], 16 * (c + 1))
                    split_unit(RING * c + r, r, not first)

            def scale_group(q, bank_set):
                act.wait_ge(s_rdeg, q + 1)
                act.wait_ge(s_taken, PAIRS + q)
                for b in range(UI):
                    last = nc.scalar.activation(scaled[:, b, :], banks[:, bank_set * UI + b, 0:F], ACT.Copy,
                                                scale=deg[:, 1, b:b + 1])
                last.then_inc(s_scaled, 1)

            def relu_group(q):
                rows = bass.ds(q * UI, UI)
                act.wait_ge(s_taken, PAIRS + q + 1)
                nc.scalar.activation(self_sb[:, rows, :], self_sb[:, rows, :], ACT.Relu).then_inc(s_relu, 1)

            def group(q, bank_set, first=False):
                split_high(CHUNKS * q, first)
                if not first:
                    scale_group(q - 1, 1 - bank_set)
                split_high(CHUNKS * q + 1)
                split_high(CHUNKS * q + 2)
                if not first:
                    relu_group(q - 1)
                for c in range(3, CHUNKS):
                    split_high(CHUNKS * q + c)

            group(0, 0, first=True)
            group(1, 1)
            with act.Fori(1, Q // SETS) as n:
                for s in range(SETS):
                    group(SETS * n + s, s)

        @block.vector
        def _(dve):
            def statistics(quad, between=None, first=False):
                if not first:
                    dve.wait_ge(s_mv, quad)
                for t in range(4):
                    last = nc.vector.bn_stats(stats[:, t, :],
                                              x_sb[:, bass.ds(4 * quad + t, 1), :].rearrange("p a f -> p (a f)"))
                last.then_inc(s_stats, 1)
                dve.wait_ge(s_stats, quad + 1)
                if not first:
                    dve.wait_ge(s_norm, quad)
                if between:
                    between()
                for t in range(4):
                    last = nc.vector.bn_aggr(mv[:, t, :], stats[:, t, :])
                last.then_inc(s_mv, 1)

            def turned_low(p, r, slot_used=True):
                dve.wait_ge(s_hthi, p + 1)
                if slot_used:
                    dve.wait_ge(s_small, p - 3)
                nc.vector.tensor_tensor(ht_lo[r % 4], turned[r % 2].rearrange("p (a k i) -> p a k i", a=2, k=KC),
                                        ht_hi[r % 4].bitcast(F32), ALU.subtract).then_inc(s_htlo, 1)

            def g_low(p, r):
                tiles = bass.ds(2 * p, 2)
                dve.wait_ge(s_ghi, p + 1)
                nc.vector.tensor_tensor(g_sb[:, tiles, GW:GC], small[r % 2][:, :, 0:F],
                                        g_sb[:, tiles, 0:F].bitcast(F32), ALU.subtract).then_inc(s_taken, 1)

            def split_unit(u, r, slot_used):
                dve.wait_ge(s_hi, u + 1)
                if slot_used:
                    dve.wait_ge(s_used, u - RING + 1)
                nc.vector.tensor_tensor(adj_lo[:, r, :, :], adj_raw[:, r, :, :],
                                        adj_hi[:, r, :, :].bitcast(F32), ALU.subtract).then_inc(s_lo, 1)

            def step(p, r, quad=None, slot_used=True, early_unit=None):
                if early_unit is not None:
                    split_unit(early_unit, early_unit, False)
                elif quad is not None:
                    statistics(quad, lambda: turned_low(p + 2, r + 2, slot_used))
                else:
                    turned_low(p + 2, r + 2, slot_used)
                g_low(p, r)

            dve.wait_ge(s_x[0], 16)
            statistics(0, first=True)
            dve.wait_ge(s_x[1], 16)
            statistics(1)
            dve.wait_ge(s_whi, 1)
            nc.vector.tensor_tensor(w_lo[:, :, :, :], w_raw[:, :, :, :], w_hi[:, :, :, :].bitcast(F32),
                                    ALU.subtract).then_inc(s_wlo, 1)
            turned_low(0, 0, slot_used=False)
            turned_low(1, 1, slot_used=False)
            dve.wait_ge(s_x[2], 16)
            statistics(2)
            dve.wait_ge(s_b, 32)
            nc.vector.tensor_tensor(b_sum[:, 0, :], b_raw[:, 0, :], b_raw[:, 1, :], ALU.add).then_inc(s_bsum, 1)

            step(0, 0, slot_used=False)
            step(1, 1, quad=3, slot_used=False)
            step(2, 2)
            dve.wait_ge(s_x[3], 16)
            with dve.Fori(1, PAIRS // 4 - 1) as n:
                step(4 * n - 1, 3, quad=2 * n + 2)
                step(4 * n, 0)
                step(4 * n + 1, 1, quad=2 * n + 3)
                step(4 * n + 2, 2)
            step(PAIRS - 5, 3)
            step(PAIRS - 4, 0)
            step(PAIRS - 3, 1)
            step(PAIRS - 2, 2, early_unit=0)
            step(PAIRS - 1, 3, early_unit=1)

            def split_low(c, first=False):
                for r in range(2 if first else 0, RING):
                    split_unit(RING * c + r, r, not first)

            def degrees(q, bank_set, first=False):
                dve.wait_ge(s_used, U * (q + 1))
                nc.vector.tensor_scalar(deg[:, 0, :], banks[:, bank_set * UI:(bank_set + 1) * UI, F], DEG_EPS,
                                        None, ALU.add).then_inc(s_deg, 1)
                dve.wait_ge(s_deg, q + 1)
                if not first:
                    dve.wait_ge(s_scaled, q)
                nc.vector.reciprocal(deg[:, 1, :], deg[:, 0, :]).then_inc(s_rdeg, 1)

            def add_self(q):
                rows = bass.ds(q * UI, UI)
                dve.wait_ge(s_scaled, q + 1)
                nc.vector.tensor_tensor(self_sb[:, rows, :], self_sb[:, rows, :], scaled, ALU.add) \
                  .then_inc(s_taken, 1)

            def group(q, bank_set, first=False, second=False):
                split_low(CHUNKS * q, first)
                if not first:
                    degrees(q - 1, 1 - bank_set, first=second)
                split_low(CHUNKS * q + 1)
                if not first:
                    add_self(q - 1)
                for c in range(2, CHUNKS):
                    split_low(CHUNKS * q + c)

            group(0, 0, first=True)
            dve.wait_ge(s_self, PAIRS)
            group(1, 1, second=True)
            with dve.Fori(1, Q // SETS) as n:
                for s in range(SETS):
                    group(SETS * n + s, s)

            for b in range(UI):
                t = (Q - 1) * UI + b
                bank = banks[:, (SETS - 1) * UI + b, :]
                if b < UI - 1:
                    dve.wait_ge(s_bank, (UI - 1) * (Q - 1) + b + 1)
                else:
                    dve.wait_ge(s_used, U * Q)
                nc.vector.tensor_scalar(deg[:, 0, b:b + 1], bank[:, F:F + 1], DEG_EPS, None, ALU.add).then_inc(s_last, 1)
                dve.wait_ge(s_last, 4 * b + 1)
                nc.vector.reciprocal(deg[:, 1, b:b + 1], deg[:, 0, b:b + 1]).then_inc(s_last, 1)
                dve.wait_ge(s_last, 4 * b + 2)
                nc.vector.scalar_tensor_tensor(out=self_sb[:, t, :], in0=bank[:, 0:F], scalar=deg[:, 1, b:b + 1],
                                               in1=self_sb[:, t, :], op0=ALU.mult, op1=ALU.add).then_inc(s_last, 1)
                dve.wait_ge(s_last, 4 * b + 3)
                nc.vector.scalar_tensor_tensor(out=x_sb[:, t, :], in0=self_sb[:, t, :], scalar=0.0,
                                               in1=x_sb[:, t, :], op0=ALU.max, op1=ALU.add).then_inc(s_last, 1)

        @block.tensor
        def _(pe):
            def turn(p, r, slot_used=True):
                pe.wait_ge(s_h, p + 1)
                if slot_used:
                    pe.wait_ge(s_htlo, p - 1)
                for t in range(2):
                    for k in range(KC):
                        at = (t * KC + k) * P
                        last = nc.tensor.transpose(turned[r % 2][:, at:at + P],
                                                   h_sb[:, r % 2, t, k * P:(k + 1) * P], ident[:, :])
                last.then_inc(s_turned, 1)

            def small_product(p, r, slot_used=True):
                pe.wait_ge(s_htlo, p + 1)
                if slot_used:
                    pe.wait_ge(s_taken, p - 1)
                terms = [(h[r % 4], w, k) for k in range(KC)
                         for h, w in ((ht_hi, w_hi), (ht_hi, w_lo), (ht_lo, w_hi))]
                for t in range(2):
                    for n, (h, w, k) in enumerate(terms):
                        last = nc.tensor.matmul(small[r % 2][:, t, :], h[:, t, k, :],
                                                w[:, k, :, :].rearrange("p a f -> p (a f)"),
                                                start=(n == 0), stop=(n == len(terms) - 1))
                last.then_inc(s_small, 1)

            def prepare(first_pair, position):
                for r in range(4):
                    p = first_pair + r
                    if position == "first" and r == 0:
                        small_product(p, r, slot_used=False)
                        turn(p + 2, r + 2)
                        continue
                    if position != "last" or r + 2 < 4:
                        turn(p + 2, r + 2)
                    small_product(p, r, slot_used=position != "first" or r >= 2)

            pe.wait_ge(s_ident, 1)
            turn(0, 0, slot_used=False)
            turn(1, 1, slot_used=False)
            pe.wait_ge(s_wlo, 1)
            prepare(0, "first")
            with pe.Fori(1, PAIRS // 4 - 1) as n:
                prepare(4 * n, "middle")
            prepare(PAIRS - 4, "last")

            def add_units(c, k, bank_set, first=False, last=False):
                for r in range(RING):
                    pe.wait_ge(s_lo, RING * c + r + 1)
                    for b in range(UI):
                        bank = banks[:, bank_set * UI + b, :]
                        for a in range(UJ):
                            j = bass.ds((RING * k + r) * UJ + a, 1)
                            g_hi = g_sb[:, j, 0:GW].rearrange("p a f -> p (a f)")
                            g_lo = g_sb[:, j, GW:GC].rearrange("p a f -> p (a f)")
                            hi = adj_hi[:, r, a, b * P:(b + 1) * P]
                            lo = adj_lo[:, r, a, b * P:(b + 1) * P]
                            start = first and r == 0 and a == 0
                            nc.tensor.matmul(bank[:, 0:GW], hi, g_hi, start=start, stop=False)
                            nc.tensor.matmul(bank[:, 0:F], hi, g_lo, start=False, stop=False)
                            stop = last and r == RING - 1 and a == UJ - 1
                            product = nc.tensor.matmul(bank[:, 0:GW], lo, g_hi, start=False, stop=stop)
                        if last and r == RING - 1 and b < UI - 1:
                            product.then_inc(s_bank, 1)
                    product.then_inc(s_used, 1)

            pe.wait_ge(s_ones, 1)
            with pe.Fori(0, Q // SETS) as n:
                for s in range(SETS):
                    q = SETS * n + s
                    pe.wait_ge(s_taken, PAIRS + q - 1)
                    add_units(CHUNKS * q, 0, s, first=True)
                    pe.wait_ge(s_taken, PAIRS)
                    with pe.Fori(1, CHUNKS - 1) as k:
                        add_units(CHUNKS * q + k, k, s)
                    add_units(CHUNKS * (q + 1) - 1, CHUNKS - 1, s, last=True)


def kernel(x, adj, L0_gnn_W_neigh, L0_gnn_b_neigh, L0_gnn_W_self, L0_gnn_b_self):
    import numpy as np
    import concourse.bacc as bacc
    from concourse.bass_utils import run_bass_kernel_spmd

    x, adj, wn, bn, ws, bs = (np.asarray(a) for a in (
        x, adj, L0_gnn_W_neigh, L0_gnn_b_neigh, L0_gnn_W_self, L0_gnn_b_self))
    N, F = x.shape
    T, Q, U = N // P, N // (UI * P), N // (UJ * P)

    def turned_weights(w):
        return w.T.reshape(F // P, P, F).transpose(1, 0, 2)

    arrays = {
        "x_in": x.reshape(T, P, F).transpose(1, 0, 2),
        "adj_in": adj.reshape(Q, UI * P, U, UJ, P).transpose(0, 2, 4, 3, 1),
        "w_neigh": turned_weights(wn),
        "w_self": turned_weights(ws),
        "b_neigh": bn.reshape(1, F),
        "b_self": bs.reshape(1, F),
    }
    arrays = {name: np.ascontiguousarray(a) for name, a in arrays.items()}
    nc = bacc.Bacc("TRN2", target_bir_lowering=False, num_devices=1)
    args = [nc.dram_tensor(name, a.shape, mybir.dt.from_np(a.dtype), kind="ExternalInput").ap()
            for name, a in arrays.items()]
    args.append(nc.dram_tensor("rows_out", (P, T, F), F32, kind="ExternalOutput").ap())
    gnn_layer(nc, *args)
    result = run_bass_kernel_spmd(nc, [arrays], core_ids=[0])
    rows = result.results[0]["rows_out"]
    return np.ascontiguousarray(rows.transpose(1, 0, 2)).reshape(N, F)
```

```python
from contextlib import ExitStack

import concourse.bass as bass
from concourse import mybir


P = 128
ALU = mybir.AluOpType
ACT = mybir.ActivationFunctionType
F32 = mybir.dt.float32
F32R = mybir.dt.float32r

LN_EPS = 1e-5
DEG_EPS = 1e-5

RING = 4
UJ = 2
UI = 4
SETS = 2


def gnn_layer(nc, x, adj, wn, ws, bn, bs, out):
    _, T, F = x.shape
    Q, U, _, _, _ = adj.shape
    KC = F // P
    PAIRS = T // 2
    QUADS = T // 4
    GW = F + 2
    GC = GW + F
    CHUNKS = U // RING
    assert U * UJ == T and Q * UI == T and U % RING == 0 and F == 2 * P

    with ExitStack() as ctx:
        def sb(name, shape, dt=F32):
            return ctx.enter_context(nc.sbuf_tensor(name, shape, dt))

        def sem(name):
            return ctx.enter_context(nc.semaphore(name))

        x_sb = sb("x_sb", [P, T, F])
        self_sb = sb("self_sb", [P, T, F])
        g_sb = sb("g_sb", [P, T, GC], F32R)
        adj_raw = sb("adj_raw", [P, RING, UJ, UI * P])
        adj_hi = sb("adj_hi", [P, RING, UJ, UI * P], F32R)
        adj_lo = sb("adj_lo", [P, RING, UJ, UI * P], F32R)
        w_raw = sb("w_raw", [P, KC, 2, F])
        w_hi = sb("w_hi", [P, KC, 2, F], F32R)
        w_lo = sb("w_lo", [P, KC, 2, F], F32R)
        h_sb = sb("h_sb", [P, 2, 2, F])
        scaled = h_sb[:, :, :, :].rearrange("p a b f -> p (a b) f")
        ht_hi, ht_lo = ([ring[:, RING // 2 + s // 2, s % 2, :].rearrange("p (a k i) -> p a k i", a=2, k=KC)
                         for s in range(4)] for ring in (adj_hi, adj_lo))
        ident = sb("ident", [P, P])
        b_raw = sb("b_raw", [P, 2, F])
        b_sum = sb("b_sum", [P, 1, F])
        stats = sb("stats", [P, 4, 6])
        mv = sb("mv", [P, 4, 2])
        rstd = sb("rstd", [P, T])
        shift = sb("shift", [P, T])
        consts = sb("consts", [P, 3, 4])
        deg = sb("deg", [P, 2, UI])

        banks = ctx.enter_context(nc.psum_tensor("banks", [P, SETS * UI, 512], F32))
        turned = [banks[:, s, :] for s in range(2)]
        small = [banks[:, UI + 2 * s:UI + 2 * s + 2, :] for s in range(2)]

        x_parts = [(0, 2), (2, 4), (4, 8), (8, 16), (16, T)]
        s_x = [sem(f"x_loaded{n}") for n in range(len(x_parts))]
        s_w = sem("w_loaded")
        s_b = sem("b_loaded")
        s_raw = [sem(f"adj_raw_loaded{r}") for r in range(RING)]
        s_zero = sem("ident_zeroed")
        s_ident = sem("ident_ready")
        s_ones = sem("ones_ready")
        s_whi = sem("w_hi_ready")
        s_wlo = sem("w_lo_ready")
        s_bsum = sem("b_sum_ready")
        s_stats = sem("stats_done")
        s_mv = sem("mv_done")
        s_consts = sem("consts_ready")
        s_rstd = sem("rstd_step_done")
        s_shift = sem("shift_step_done")
        s_norm = sem("norm_ready")
        s_h = sem("h_ready")
        s_turned = sem("h_turned")
        s_hthi = sem("ht_hi_ready")
        s_htlo = sem("ht_lo_ready")
        s_small = sem("small_product_done")
        s_results = sem("g_hi_and_self_ready")
        s_self = sem("self_with_bias")
        s_taken = sem("results_taken")
        s_hi = sem("adj_hi_ready")
        s_lo = sem("adj_lo_ready")
        s_used = sem("adj_unit_used")
        s_bank = sem("bank_complete")
        s_deg = sem("deg_ready")
        s_rdeg = sem("rdeg_ready")
        s_scaled = sem("scaled_ready")
        s_relu = sem("relu_ready")
        s_final = sem("rows_final")
        s_last = sem("last_group_step")
        s_out = sem("out_stored")
        s_tail = sem("last_group_stored")

        block = ctx.enter_context(nc.Block())

        @block.sync
        def _(sp):
            def load_x(n):
                a, b = x_parts[n]
                sp.dma_start(x_sb[:, a:b, :], x[:, a:b, :]).then_inc(s_x[n], 16)

            def load_units(c, ring_full):
                for r in range(RING):
                    if ring_full:
                        sp.wait_ge(s_hi, RING * c + r - RING + 1)
                        sp.wait_ge(s_lo, RING * c + r - RING + 1)
                    sp.dma_start(adj_raw[:, r, :, :],
                                 adj_units[bass.ds(RING * c + r, 1), :, :, :].rearrange("u p a i -> p (u a) i")) \
                      .then_inc(s_raw[r], 16)

            adj_units = adj.rearrange("q u p a i -> (q u) p a i")
            load_x(0)
            sp.dma_start(w_raw[:, :, 0, :], wn).then_inc(s_w, 16)
            sp.dma_start(w_raw[:, :, 1, :], ws).then_inc(s_w, 16)
            load_x(1)
            load_x(2)
            sp.dma_start(b_raw[:, 0, :], bn.broadcast_to([P, F])).then_inc(s_b, 16)
            sp.dma_start(b_raw[:, 1, :], bs.broadcast_to([P, F])).then_inc(s_b, 16)
            load_x(3)
            load_x(4)
            load_units(0, False)
            with sp.Fori(1, Q * U // RING) as c:
                load_units(c, True)
            for a, b in ((0, UI - 1), (UI - 1, UI)):
                rows = slice((Q - 1) * UI + a, (Q - 1) * UI + b)
                sp.wait_ge(s_last, 4 * b)
                sp.dma_start(out[:, rows, :], x_sb[:, rows, :]).then_inc(s_tail, 16)
            sp.wait_ge(s_tail, 32)

        @block.gpsimd
        def _(pool):
            nc.gpsimd.memset(ident[:, :], 0.0).then_inc(s_zero, 1)
            pool.wait_ge(s_zero, 1)
            nc.gpsimd.affine_select(out=ident[:, :], in_=ident[:, :], compare_op=ALU.not_equal, fill=1.0,
                                    base=0, pattern=[[-1, P]], channel_multiplier=1).then_inc(s_ident, 1)
            nc.gpsimd.memset(g_sb[:, :, F:GW].bitcast(F32), 1.0).then_inc(s_ones, 1)

            for n, value in enumerate((LN_EPS, -0.5, -1.0)):
                nc.gpsimd.memset(consts[:, n, :], value).then_inc(s_consts, 1)
            pool.wait_ge(s_consts, 3)

            def norm(count, first, tiles=4):
                cols = slice(first, first + tiles)
                mean, var = mv[:, 0:tiles, 0], mv[:, 0:tiles, 1]
                pool.wait_ge(s_mv, count + 1)
                nc.gpsimd.tensor_tensor(rstd[:, cols], var, consts[:, 0, 0:tiles], ALU.add).then_inc(s_rstd, 1)
                nc.gpsimd.tensor_tensor(shift[:, cols], mean, consts[:, 2, 0:tiles], ALU.mult).then_inc(s_shift, 1)
                pool.wait_ge(s_rstd, 2 * count + 1)
                nc.gpsimd.tensor_tensor(rstd[:, cols], rstd[:, cols], consts[:, 1, 0:tiles], ALU.pow) \
                  .then_inc(s_rstd, 1)
                pool.wait_ge(s_rstd, 2 * count + 2)
                pool.wait_ge(s_shift, count + 1)
                nc.gpsimd.tensor_tensor(shift[:, cols], shift[:, cols], rstd[:, cols], ALU.mult).then_inc(s_norm, 1)

            norm(0, 0, tiles=2)
            norm(1, 2, tiles=2)
            norm(2, 4)
            norm(3, 8)
            for p in range(PAIRS):
                if p % 2 == 1 and (p + 5) // 2 < QUADS:
                    norm((p + 5) // 2 + 1, 4 * ((p + 5) // 2))
                tiles = slice(2 * p, 2 * p + 2)
                if p == 0:
                    pool.wait_ge(s_bsum, 1)
                pool.wait_ge(s_results, p + 1)
                nc.gpsimd.tensor_tensor(self_sb[:, tiles, :], self_sb[:, tiles, :],
                                        b_sum[:, :, :].broadcast_to([P, 2, F]), ALU.add).then_inc(s_self, 1)

            for q in range(Q - 1):
                rows = slice(q * UI, (q + 1) * UI)
                pool.wait_ge(s_relu, q + 1)
                nc.gpsimd.tensor_tensor(x_sb[:, rows, :], x_sb[:, rows, :], self_sb[:, rows, :], ALU.add) \
                  .then_inc(s_final, 1)
                pool.wait_ge(s_final, q + 1)
                pool.dma_start(out[:, rows, :], x_sb[:, rows, :]).then_inc(s_out, 16)
            pool.wait_ge(s_out, 16 * (Q - 1))

        @block.scalar
        def _(act):
            def normalise(p, r, norms, slot_used=True):
                act.wait_ge(s_norm, norms)
                if slot_used:
                    act.wait_ge(s_turned, p - 1)
                for t in range(2):
                    col = bass.ds(2 * p + t, 1)
                    last = nc.scalar.activation(h_sb[:, r % 2, t, :],
                                                x_sb[:, col, :].rearrange("p a f -> p (a f)"),
                                                ACT.Relu, bias=shift[:, col], scale=rstd[:, col])
                last.then_inc(s_h, 1)

            def turned_high(p, r, slot_used=True):
                act.wait_ge(s_turned, p + 1)
                if slot_used:
                    act.wait_ge(s_small, p - 3)
                nc.scalar.activation(ht_hi[r % 4], turned[r % 2].rearrange("p (a k i) -> p a k i", a=2, k=KC),
                                     ACT.Copy).then_inc(s_hthi, 1)

            def results(p, r):
                tiles = bass.ds(2 * p, 2)
                act.wait_ge(s_small, p + 1)
                nc.scalar.activation(g_sb[:, tiles, 0:F], small[r % 2][:, :, 0:F], ACT.Copy)
                nc.scalar.activation(self_sb[:, tiles, :], small[r % 2][:, :, F:2 * F], ACT.Copy).then_inc(s_results, 1)

            def split_unit(u, r, slot_used):
                if slot_used:
                    act.wait_ge(s_used, u - RING + 1)
                nc.scalar.activation(adj_hi[:, r, :, :], adj_raw[:, r, :, :], ACT.Copy).then_inc(s_hi, 1)

            act.wait_ge(s_w, 32)
            nc.scalar.activation(w_hi[:, :, :, :], w_raw[:, :, :, :], ACT.Copy).then_inc(s_whi, 1)
            normalise(0, 0, 1, slot_used=False)
            turned_high(0, 0, slot_used=False)
            normalise(1, 1, 2, slot_used=False)
            turned_high(1, 1, slot_used=False)
            normalise(2, 2, 3)

            def prepare(first_pair, position):
                for r in range(4):
                    p = first_pair + r
                    if position != "last" or r + 3 < 4:
                        normalise(p + 3, r + 3, first_pair // 2 + (r + 3) // 2 + 2)
                    if position != "last" or r + 2 < 4:
                        turned_high(p + 2, r + 2, slot_used=position != "first" or r + 2 >= 4)
                    else:
                        u = r - 2
                        act.wait_ge(s_raw[u], 16)
                        split_unit(u, u, False)
                    results(p, r)

            prepare(0, "first")
            with act.Fori(1, PAIRS // 4 - 1) as n:
                prepare(4 * n, "middle")
            prepare(PAIRS - 4, "last")

            def split_high(c, first=False):
                for r in range(2 if first else 0, RING):
                    act.wait_ge(s_raw[r], 16 * (c + 1))
                    split_unit(RING * c + r, r, not first)

            def scale_group(q, bank_set):
                act.wait_ge(s_rdeg, q + 1)
                act.wait_ge(s_taken, PAIRS + q)
                for b in range(UI):
                    last = nc.scalar.activation(scaled[:, b, :], banks[:, bank_set * UI + b, 0:F], ACT.Copy,
                                                scale=deg[:, 1, b:b + 1])
                last.then_inc(s_scaled, 1)

            def relu_group(q):
                rows = bass.ds(q * UI, UI)
                act.wait_ge(s_taken, PAIRS + q + 1)
                nc.scalar.activation(self_sb[:, rows, :], self_sb[:, rows, :], ACT.Relu).then_inc(s_relu, 1)

            def group(q, bank_set, first=False):
                split_high(CHUNKS * q, first)
                if not first:
                    scale_group(q - 1, 1 - bank_set)
                split_high(CHUNKS * q + 1)
                split_high(CHUNKS * q + 2)
                if not first:
                    relu_group(q - 1)
                for c in range(3, CHUNKS):
                    split_high(CHUNKS * q + c)

            group(0, 0, first=True)
            group(1, 1)
            with act.Fori(1, Q // SETS) as n:
                for s in range(SETS):
                    group(SETS * n + s, s)

        @block.vector
        def _(dve):
            def statistics(count, first, between=None, tiles=4, earlier=True):
                if earlier:
                    dve.wait_ge(s_mv, count)
                for t in range(tiles):
                    last = nc.vector.bn_stats(stats[:, t, :],
                                              x_sb[:, bass.ds(first + t, 1), :].rearrange("p a f -> p (a f)"))
                last.then_inc(s_stats, 1)
                dve.wait_ge(s_stats, count + 1)
                if earlier:
                    dve.wait_ge(s_norm, count)
                if between:
                    between()
                for t in range(tiles):
                    last = nc.vector.bn_aggr(mv[:, t, :], stats[:, t, :])
                last.then_inc(s_mv, 1)

            def turned_low(p, r, slot_used=True):
                dve.wait_ge(s_hthi, p + 1)
                if slot_used:
                    dve.wait_ge(s_small, p - 3)
                nc.vector.tensor_tensor(ht_lo[r % 4], turned[r % 2].rearrange("p (a k i) -> p a k i", a=2, k=KC),
                                        ht_hi[r % 4].bitcast(F32), ALU.subtract).then_inc(s_htlo, 1)

            def g_low(p, r):
                tiles = bass.ds(2 * p, 2)
                dve.wait_ge(s_results, p + 1)
                nc.vector.tensor_tensor(g_sb[:, tiles, GW:GC], small[r % 2][:, :, 0:F],
                                        g_sb[:, tiles, 0:F].bitcast(F32), ALU.subtract).then_inc(s_taken, 1)

            def split_unit(u, r, slot_used):
                dve.wait_ge(s_hi, u + 1)
                if slot_used:
                    dve.wait_ge(s_used, u - RING + 1)
                nc.vector.tensor_tensor(adj_lo[:, r, :, :], adj_raw[:, r, :, :],
                                        adj_hi[:, r, :, :].bitcast(F32), ALU.subtract).then_inc(s_lo, 1)

            def step(p, r, quad=None, slot_used=True, early_unit=None):
                if early_unit is not None:
                    split_unit(early_unit, early_unit, False)
                elif quad is not None:
                    statistics(quad + 1, 4 * quad, lambda: turned_low(p + 2, r + 2, slot_used))
                else:
                    turned_low(p + 2, r + 2, slot_used)
                g_low(p, r)

            dve.wait_ge(s_x[0], 16)
            statistics(0, 0, tiles=2, earlier=False)
            dve.wait_ge(s_x[1], 16)
            statistics(1, 2, tiles=2)
            dve.wait_ge(s_whi, 1)
            nc.vector.tensor_tensor(w_lo[:, :, :, :], w_raw[:, :, :, :], w_hi[:, :, :, :].bitcast(F32),
                                    ALU.subtract).then_inc(s_wlo, 1)
            turned_low(0, 0, slot_used=False)
            dve.wait_ge(s_x[2], 16)
            statistics(2, 4)
            turned_low(1, 1, slot_used=False)
            dve.wait_ge(s_x[3], 16)
            statistics(3, 8)
            dve.wait_ge(s_b, 32)
            nc.vector.tensor_tensor(b_sum[:, 0, :], b_raw[:, 0, :], b_raw[:, 1, :], ALU.add).then_inc(s_bsum, 1)

            step(0, 0, slot_used=False)
            step(1, 1, quad=3, slot_used=False)
            step(2, 2)
            dve.wait_ge(s_x[4], 16)
            with dve.Fori(1, PAIRS // 4 - 1) as n:
                step(4 * n - 1, 3, quad=2 * n + 2)
                step(4 * n, 0)
                step(4 * n + 1, 1, quad=2 * n + 3)
                step(4 * n + 2, 2)
            step(PAIRS - 5, 3)
            step(PAIRS - 4, 0)
            step(PAIRS - 3, 1)
            step(PAIRS - 2, 2, early_unit=0)
            step(PAIRS - 1, 3, early_unit=1)

            def split_low(c, first=False):
                for r in range(2 if first else 0, RING):
                    split_unit(RING * c + r, r, not first)

            def degrees(q, bank_set, first=False):
                dve.wait_ge(s_used, U * (q + 1))
                nc.vector.tensor_scalar(deg[:, 0, :], banks[:, bank_set * UI:(bank_set + 1) * UI, F], DEG_EPS,
                                        None, ALU.add).then_inc(s_deg, 1)
                dve.wait_ge(s_deg, q + 1)
                if not first:
                    dve.wait_ge(s_scaled, q)
                nc.vector.reciprocal(deg[:, 1, :], deg[:, 0, :]).then_inc(s_rdeg, 1)

            def add_self(q):
                rows = bass.ds(q * UI, UI)
                dve.wait_ge(s_scaled, q + 1)
                nc.vector.tensor_tensor(self_sb[:, rows, :], self_sb[:, rows, :], scaled, ALU.add) \
                  .then_inc(s_taken, 1)

            def group(q, bank_set, first=False, second=False):
                split_low(CHUNKS * q, first)
                if not first:
                    degrees(q - 1, 1 - bank_set, first=second)
                split_low(CHUNKS * q + 1)
                if not first:
                    add_self(q - 1)
                for c in range(2, CHUNKS):
                    split_low(CHUNKS * q + c)

            group(0, 0, first=True)
            dve.wait_ge(s_self, PAIRS)
            group(1, 1, second=True)
            with dve.Fori(1, Q // SETS) as n:
                for s in range(SETS):
                    group(SETS * n + s, s)

            for b in range(UI):
                t = (Q - 1) * UI + b
                bank = banks[:, (SETS - 1) * UI + b, :]
                if b < UI - 1:
                    dve.wait_ge(s_bank, (UI - 1) * (Q - 1) + b + 1)
                else:
                    dve.wait_ge(s_used, U * Q)
                nc.vector.tensor_scalar(deg[:, 0, b:b + 1], bank[:, F:F + 1], DEG_EPS, None, ALU.add).then_inc(s_last, 1)
                dve.wait_ge(s_last, 4 * b + 1)
                nc.vector.reciprocal(deg[:, 1, b:b + 1], deg[:, 0, b:b + 1]).then_inc(s_last, 1)
                dve.wait_ge(s_last, 4 * b + 2)
                nc.vector.scalar_tensor_tensor(out=self_sb[:, t, :], in0=bank[:, 0:F], scalar=deg[:, 1, b:b + 1],
                                               in1=self_sb[:, t, :], op0=ALU.mult, op1=ALU.add).then_inc(s_last, 1)
                dve.wait_ge(s_last, 4 * b + 3)
                nc.vector.scalar_tensor_tensor(out=x_sb[:, t, :], in0=self_sb[:, t, :], scalar=0.0,
                                               in1=x_sb[:, t, :], op0=ALU.max, op1=ALU.add).then_inc(s_last, 1)

        @block.tensor
        def _(pe):
            def turn(p, r, slot_used=True):
                pe.wait_ge(s_h, p + 1)
                if slot_used:
                    pe.wait_ge(s_htlo, p - 1)
                for t in range(2):
                    for k in range(KC):
                        at = (t * KC + k) * P
                        last = nc.tensor.transpose(turned[r % 2][:, at:at + P],
                                                   h_sb[:, r % 2, t, k * P:(k + 1) * P], ident[:, :])
                last.then_inc(s_turned, 1)

            def small_product(p, r, slot_used=True):
                pe.wait_ge(s_htlo, p + 1)
                if slot_used:
                    pe.wait_ge(s_taken, p - 1)
                terms = [(h[r % 4], w, k) for k in range(KC)
                         for h, w in ((ht_hi, w_hi), (ht_hi, w_lo), (ht_lo, w_hi))]
                for t in range(2):
                    for n, (h, w, k) in enumerate(terms):
                        last = nc.tensor.matmul(small[r % 2][:, t, :], h[:, t, k, :],
                                                w[:, k, :, :].rearrange("p a f -> p (a f)"),
                                                start=(n == 0), stop=(n == len(terms) - 1))
                last.then_inc(s_small, 1)

            def prepare(first_pair, position):
                for r in range(4):
                    p = first_pair + r
                    if position == "first" and r == 0:
                        small_product(p, r, slot_used=False)
                        turn(p + 2, r + 2)
                        continue
                    if position != "last" or r + 2 < 4:
                        turn(p + 2, r + 2)
                    small_product(p, r, slot_used=position != "first" or r >= 2)

            pe.wait_ge(s_ident, 1)
            turn(0, 0, slot_used=False)
            turn(1, 1, slot_used=False)
            pe.wait_ge(s_wlo, 1)
            prepare(0, "first")
            with pe.Fori(1, PAIRS // 4 - 1) as n:
                prepare(4 * n, "middle")
            prepare(PAIRS - 4, "last")

            def add_units(c, k, bank_set, first=False, last=False):
                runs = [[r] for r in range(RING - 2)] + ([[RING - 2, RING - 1]] if last else
                                                         [[RING - 2], [RING - 1]])
                for run in runs:
                    for b in range(UI):
                        bank = banks[:, bank_set * UI + b, :]
                        for r in run:
                            if b == 0:
                                pe.wait_ge(s_lo, RING * c + r + 1)
                            for a in range(UJ):
                                j = bass.ds((RING * k + r) * UJ + a, 1)
                                g_hi = g_sb[:, j, 0:GW].rearrange("p a f -> p (a f)")
                                g_lo = g_sb[:, j, GW:GC].rearrange("p a f -> p (a f)")
                                hi = adj_hi[:, r, a, b * P:(b + 1) * P]
                                lo = adj_lo[:, r, a, b * P:(b + 1) * P]
                                start = first and r == 0 and a == 0
                                stop = last and r == RING - 1 and a == UJ - 1
                                nc.tensor.matmul(bank[:, 0:GW], hi, g_hi, start=start, stop=False)
                                nc.tensor.matmul(bank[:, 0:F], hi, g_lo, start=False, stop=False)
                                product = nc.tensor.matmul(bank[:, 0:GW], lo, g_hi, start=False, stop=stop)
                            if b == UI - 1:
                                product.then_inc(s_used, 1)
                        if last and run[-1] == RING - 1 and b < UI - 1:
                            product.then_inc(s_bank, 1)

            pe.wait_ge(s_ones, 1)
            with pe.Fori(0, Q // SETS) as n:
                for s in range(SETS):
                    q = SETS * n + s
                    pe.wait_ge(s_taken, PAIRS + q - 1)
                    add_units(CHUNKS * q, 0, s, first=True)
                    pe.wait_ge(s_taken, PAIRS)
                    with pe.Fori(1, CHUNKS - 1) as k:
                        add_units(CHUNKS * q + k, k, s)
                    add_units(CHUNKS * (q + 1) - 1, CHUNKS - 1, s, last=True)


def kernel(x, adj, L0_gnn_W_neigh, L0_gnn_b_neigh, L0_gnn_W_self, L0_gnn_b_self):
    import numpy as np
    import concourse.bacc as bacc
    from concourse.bass_utils import run_bass_kernel_spmd

    x, adj, wn, bn, ws, bs = (np.asarray(a) for a in (
        x, adj, L0_gnn_W_neigh, L0_gnn_b_neigh, L0_gnn_W_self, L0_gnn_b_self))
    N, F = x.shape
    T, Q, U = N // P, N // (UI * P), N // (UJ * P)

    def turned_weights(w):
        return w.T.reshape(F // P, P, F).transpose(1, 0, 2)

    arrays = {
        "x_in": x.reshape(T, P, F).transpose(1, 0, 2),
        "adj_in": adj.reshape(Q, UI * P, U, UJ, P).transpose(0, 2, 4, 3, 1),
        "w_neigh": turned_weights(wn),
        "w_self": turned_weights(ws),
        "b_neigh": bn.reshape(1, F),
        "b_self": bs.reshape(1, F),
    }
    arrays = {name: np.ascontiguousarray(a) for name, a in arrays.items()}
    nc = bacc.Bacc("TRN2", target_bir_lowering=False, num_devices=1)
    args = [nc.dram_tensor(name, a.shape, mybir.dt.from_np(a.dtype), kind="ExternalInput").ap()
            for name, a in arrays.items()]
    args.append(nc.dram_tensor("rows_out", (P, T, F), F32, kind="ExternalOutput").ap())
    gnn_layer(nc, *args)
    result = run_bass_kernel_spmd(nc, [arrays], core_ids=[0])
    rows = result.results[0]["rows_out"]
    return np.ascontiguousarray(rows.transpose(1, 0, 2)).reshape(N, F)
```
